# Optimizing a Trainium2 kernel written in Bass

```python
import numpy as np
import jax
import jax.numpy as jnp

def _softmax(x, axis=-1):
    return jax.nn.softmax(x, axis=axis)

def _gelu(x):
    return jax.nn.gelu(x, approximate=True)

def _silu(x):
    return jax.nn.silu(x)

def _sigmoid(x):
    return jax.nn.sigmoid(x)

def _layernorm(x, axis=-1, eps=1e-05):
    m = jnp.mean(x, axis=axis, keepdims=True)
    v = jnp.var(x, axis=axis, keepdims=True)
    return (x - m) / jnp.sqrt(v + eps)

def _scatter_add(tgt, idx, src, axis=0):
    return tgt.at[idx].add(src)

def _segment_sum(src, seg, n):
    return jax.ops.segment_sum(src, seg, n)
kernel_name = 'mk_rec_standalone_d1_rec_r8_72dab2'

def setup_inputs(seed: int=0):
    np.random.seed(seed)
    _w = jnp.asarray

    def _rec_inputs():
        import jax
        import jax.numpy as jnp
        _rk = jax.random.key(seed)
        r_categorical_input = jnp.stack([jax.random.randint(jax.random.fold_in(jax.random.fold_in(_rk, 1), 0), (2048,), 0, 99999, jnp.int32), jax.random.randint(jax.random.fold_in(jax.random.fold_in(_rk, 1), 1), (2048,), 0, 12499, jnp.int32), jax.random.randint(jax.random.fold_in(jax.random.fold_in(_rk, 1), 2), (2048,), 4, 99997, jnp.int32), jax.random.randint(jax.random.fold_in(jax.random.fold_in(_rk, 1), 3), (2048,), 2, 99997, jnp.int32), jax.random.randint(jax.random.fold_in(jax.random.fold_in(_rk, 1), 4), (2048,), 1, 99988, jnp.int32), jax.random.randint(jax.random.fold_in(jax.random.fold_in(_rk, 1), 5), (2048,), 1, 99996, jnp.int32), jax.random.randint(jax.random.fold_in(jax.random.fold_in(_rk, 1), 6), (2048,), 12, 99997, jnp.int32), jax.random.randint(jax.random.fold_in(jax.random.fold_in(_rk, 1), 7), (2048,), 17, 99995, jnp.int32), jax.random.randint(jax.random.fold_in(jax.random.fold_in(_rk, 1), 8), (2048,), 0, 99998, jnp.int32), jax.random.randint(jax.random.fold_in(jax.random.fold_in(_rk, 1), 9), (2048,), 0, 99998, jnp.int32), jax.random.randint(jax.random.fold_in(jax.random.fold_in(_rk, 1), 10), (2048,), 3, 99993, jnp.int32), jax.random.randint(jax.random.fold_in(jax.random.fold_in(_rk, 1), 11), (2048,), 0, 99993, jnp.int32), jax.random.randint(jax.random.fold_in(jax.random.fold_in(_rk, 1), 12), (2048,), 1, 99988, jnp.int32), jax.random.randint(jax.random.fold_in(jax.random.fold_in(_rk, 1), 13), (2048,), 0, 99997, jnp.int32), jax.random.randint(jax.random.fold_in(jax.random.fold_in(_rk, 1), 14), (2048,), 3, 99993, jnp.int32), jax.random.randint(jax.random.fold_in(jax.random.fold_in(_rk, 1), 15), (2048,), 10, 99994, jnp.int32), jax.random.randint(jax.random.fold_in(jax.random.fold_in(_rk, 1), 16), (2048,), 10, 99998, jnp.int32), jax.random.randint(jax.random.fold_in(jax.random.fold_in(_rk, 1), 17), (2048,), 18, 99979, jnp.int32), jax.random.randint(jax.random.fold_in(jax.random.fold_in(_rk, 1), 18), (2048,), 1, 99996, jnp.int32), jax.random.randint(jax.random.fold_in(jax.random.fold_in(_rk, 1), 19), (2048,), 6, 99987, jnp.int32), jax.random.randint(jax.random.fold_in(jax.random.fold_in(_rk, 1), 20), (2048,), 6, 12500, jnp.int32), jax.random.randint(jax.random.fold_in(jax.random.fold_in(_rk, 1), 21), (2048,), 2, 12500, jnp.int32), jax.random.randint(jax.random.fold_in(jax.random.fold_in(_rk, 1), 22), (2048,), 7, 12498, jnp.int32), jax.random.randint(jax.random.fold_in(jax.random.fold_in(_rk, 1), 23), (2048,), 2, 99999, jnp.int32), jax.random.randint(jax.random.fold_in(jax.random.fold_in(_rk, 1), 24), (2048,), 29, 99990, jnp.int32), jax.random.randint(jax.random.fold_in(jax.random.fold_in(_rk, 1), 25), (2048,), 10, 99986, jnp.int32)], axis=1)
        return r_categorical_input
    r_categorical_input = _rec_inputs()

    def _L0_rec_setup():
        import jax, jax.numpy as jnp
        import numpy as np
        B = 2048
        N_CAT = 26
        VOCAB = 12500
        EMB = 32
        NUM_NUM = 13
        D = N_CAT * EMB + NUM_NUM
        LAYER_SIZES = [1024, 512, 256]
        N_CROSS = 3
        OUT_DIM = 1

        def _forward(categorical_input, numerical_input, emb_tables, alphas, cross_bias, W1, b1, W2, b2, W3, b3, Wc, bc):
            emb = emb_tables[jnp.arange(N_CAT)[None, :], categorical_input]
            combined = jnp.concatenate([emb.reshape(B, N_CAT * EMB), numerical_input], axis=1)
            x = combined
            for l in range(N_CROSS):
                s = jnp.einsum('bd,d->b', x, alphas[l])
                x = x * s[:, None] + x + cross_bias[l][None, :]
            h = jax.nn.relu(combined @ W1 + b1)
            h = jax.nn.relu(h @ W2 + b2)
            h = h @ W3 + b3
            cat = jnp.concatenate([x, h], axis=1)
            return jax.nn.sigmoid(cat @ Wc + bc)
        key = jax.random.key(seed)
        ks = jax.random.split(key, 16)
        stdv = 1.0 / np.sqrt(D)
        inp = {'categorical_input': jax.random.randint(ks[0], (B, N_CAT), 0, VOCAB, dtype=jnp.int32), 'numerical_input': jax.random.normal(ks[1], (B, NUM_NUM), dtype=jnp.float32), 'emb_tables': jax.random.normal(ks[2], (N_CAT, VOCAB, EMB), dtype=jnp.float32) * 0.05, 'alphas': jax.random.uniform(ks[3], (N_CROSS, D), jnp.float32, -stdv, stdv), 'cross_bias': jnp.zeros((N_CROSS, D), dtype=jnp.float32), 'W1': jax.random.normal(ks[4], (D, LAYER_SIZES[0]), dtype=jnp.float32) / np.sqrt(D), 'b1': jnp.zeros((LAYER_SIZES[0],), dtype=jnp.float32), 'W2': jax.random.normal(ks[5], (LAYER_SIZES[0], LAYER_SIZES[1]), dtype=jnp.float32) / np.sqrt(LAYER_SIZES[0]), 'b2': jnp.zeros((LAYER_SIZES[1],), dtype=jnp.float32), 'W3': jax.random.normal(ks[6], (LAYER_SIZES[1], LAYER_SIZES[2]), dtype=jnp.float32) / np.sqrt(LAYER_SIZES[1]), 'b3': jnp.zeros((LAYER_SIZES[2],), dtype=jnp.float32), 'Wc': jax.random.normal(ks[7], (D + LAYER_SIZES[2], OUT_DIM), dtype=jnp.float32) / np.sqrt(D + LAYER_SIZES[2]), 'bc': jnp.zeros((OUT_DIM,), dtype=jnp.float32)}
        return inp
    _L0_rec_all = _L0_rec_setup()
    _L0_rec_in = {k: v for k, v in _L0_rec_all.items() if k in ('numerical_input', 'emb_tables', 'alphas', 'cross_bias', 'W1', 'b1', 'W2', 'b2', 'W3', 'b3', 'Wc', 'bc')}
    del _L0_rec_all
    return {'r_categorical_input': r_categorical_input, 'L0_rec_numerical_input': _L0_rec_in['numerical_input'], 'L0_rec_emb_tables': _L0_rec_in['emb_tables'], 'L0_rec_alphas': _L0_rec_in['alphas'], 'L0_rec_cross_bias': _L0_rec_in['cross_bias'], 'L0_rec_W1': _L0_rec_in['W1'], 'L0_rec_b1': _L0_rec_in['b1'], 'L0_rec_W2': _L0_rec_in['W2'], 'L0_rec_b2': _L0_rec_in['b2'], 'L0_rec_W3': _L0_rec_in['W3'], 'L0_rec_b3': _L0_rec_in['b3'], 'L0_rec_Wc': _L0_rec_in['Wc'], 'L0_rec_bc': _L0_rec_in['bc']}

def reference(r_categorical_input, L0_rec_numerical_input, L0_rec_emb_tables, L0_rec_alphas, L0_rec_cross_bias, L0_rec_W1, L0_rec_b1, L0_rec_W2, L0_rec_b2, L0_rec_W3, L0_rec_b3, L0_rec_Wc, L0_rec_bc):
    import jax
    import jax.numpy as jnp

    def _L0_rec_ref(categorical_input, numerical_input, emb_tables, alphas, cross_bias, W1, b1, W2, b2, W3, b3, Wc, bc):
        import jax, jax.numpy as jnp
        import numpy as np
        B = 2048
        N_CAT = 26
        VOCAB = 12500
        EMB = 32
        NUM_NUM = 13
        D = N_CAT * EMB + NUM_NUM
        LAYER_SIZES = [1024, 512, 256]
        N_CROSS = 3
        OUT_DIM = 1

        def _forward(categorical_input, numerical_input, emb_tables, alphas, cross_bias, W1, b1, W2, b2, W3, b3, Wc, bc):
            emb = emb_tables[jnp.arange(N_CAT)[None, :], categorical_input]
            combined = jnp.concatenate([emb.reshape(B, N_CAT * EMB), numerical_input], axis=1)
            x = combined
            for l in range(N_CROSS):
                s = jnp.einsum('bd,d->b', x, alphas[l])
                x = x * s[:, None] + x + cross_bias[l][None, :]
            h = jax.nn.relu(combined @ W1 + b1)
            h = jax.nn.relu(h @ W2 + b2)
            h = h @ W3 + b3
            cat = jnp.concatenate([x, h], axis=1)
            return jax.nn.sigmoid(cat @ Wc + bc)
        return _forward(categorical_input, numerical_input, emb_tables, alphas, cross_bias, W1, b1, W2, b2, W3, b3, Wc, bc)
    y = _L0_rec_ref(r_categorical_input, L0_rec_numerical_input, L0_rec_emb_tables, L0_rec_alphas, L0_rec_cross_bias, L0_rec_W1, L0_rec_b1, L0_rec_W2, L0_rec_b2, L0_rec_W3, L0_rec_b3, L0_rec_Wc, L0_rec_bc)
    return y

_drawn_inputs = setup_inputs


def setup_inputs(seed=0):
    import zlib

    import numpy as np

    out = dict(_drawn_inputs(seed))
    spreads = {'L0_rec_cross_bias': (0.0, 0.299),
     'L0_rec_b1': (0.0, 0.8),
     'L0_rec_b2': (0.0, 0.8),
     'L0_rec_b3': (0.0, 0.287)}
    factors = {'L0_rec_emb_tables': 3.745,
     'L0_rec_alphas': 5.623,
     'L0_rec_W1': 6.366,
     'L0_rec_W2': 6.273,
     'L0_rec_W3': 4.015}
    for name, (base, spread) in spreads.items():
        noise = np.random.default_rng([zlib.crc32(name.encode()), seed]).standard_normal(out[name].shape)
        drawn = base * np.exp(spread * noise) if base else spread * noise
        out[name] = jnp.asarray(drawn.astype(out[name].dtype))
    for name, factor in factors.items():
        out[name] = (out[name] * factor).astype(out[name].dtype)
    return out
```

```python
import concourse.bass as bass
from concourse import mybir
from contextlib import ExitStack


def deep_cross_kernel(nc, cat, num, emb, alphas, cross_bias, W1, b1, W2, b2, W3, b3, Wc, bc, out):
    fp32, i32 = mybir.dt.float32, mybir.dt.int32
    ALU = mybir.AluOpType
    ACT = mybir.ActivationFunctionType
    AX = mybir.AxisListType

    P = 128
    B, TABLES = cat.shape
    _, VOCAB, EMB = emb.shape
    NUMS = num.shape[1]
    D, H1 = W1.shape
    H2 = W2.shape[1]
    H3 = W3.shape[1]
    CROSS = alphas.shape[0]
    TILES = B // P
    PER_CHUNK = P // EMB
    CHUNKS = (D + P - 1) // P
    FULL = D // P
    LAST = D - FULL * P
    M1, M2, M3 = H1 // P, H2 // P, H3 // P
    PAIR = 2
    PAIRS = TILES // PAIR
    W = PAIR * P
    VECS = 2 * CROSS + 1
    DOTS = CROSS + 1
    BETA01, BETA02, BETA12, GAMMA0, GAMMA1, GAMMA2, B3WC = range(7)
    BIAS_DOTS = ((CROSS + 1, 1), (CROSS + 1, 2), (CROSS + 2, 2), (CROSS + 1, CROSS), (CROSS + 2, CROSS), (CROSS + 3, CROSS))

    def tables(k):
        return range(k * PER_CHUNK, min((k + 1) * PER_CHUNK, TABLES))

    def width(k):
        return P if k < FULL else LAST

    rows = emb.rearrange("t v e -> (t v) e")

    ctx = ExitStack()
    with ctx:
        def sb(name, shape, dt=fp32):
            return ctx.enter_context(nc.sbuf_tensor(name, shape, dt))

        def pb(name, shape):
            return ctx.enter_context(nc.psum_tensor(name, shape, fp32))

        def sem(name):
            return ctx.enter_context(nc.semaphore(name))

        cat_sb = sb("cat_sb", [P, TILES, TABLES], i32)
        num_sb = sb("num_sb", [P, TILES, NUMS])
        vec_rows = sb("vec_rows", [VECS, D])
        bias_rows = sb("bias_rows", [M1 + M2 + 2 * M3, P])
        w1_sb = sb("w1_sb", [P, CHUNKS, H1])
        w2_sb = sb("w2_sb", [P, M1, H2])
        w3_sb = sb("w3_sb", [P, M2, H3])
        wch_bc = sb("wch_bc", [P, H3])
        b2_row = sb("b2_row", [1, H2])
        bc_bc = sb("bc_bc", [P, 1])
        ident = sb("ident", [P, P])
        ones = sb("ones", [P, P])
        table_base = sb("table_base", [P, TILES, TABLES])
        vecs = sb("vecs", [P, CHUNKS, VECS])
        bias_cols = sb("bias_cols", [P, M1 + M2 + 2 * M3])
        bias_prod = sb("bias_prod", [P, 7, CHUNKS])
        bias_part = sb("bias_part", [P, 7])
        cst = sb("cst", [P, 8])
        w3_prod = sb("w3_prod", [P, M2, H3])
        head = sb("head", [P, M2])
        head_diag = sb("head_diag", [P, M2, P])
        head_bc = sb("head_bc", [P, H2])
        clipped = sb("clipped", [P, TILES, TABLES])
        wrap = sb("wrap", [P, TILES, TABLES])
        idx_all = sb("idx_all", [P, TILES, TABLES], i32)
        idx = sb("idx", [P, PAIR, TABLES], i32)
        x = sb("x", [P, PAIR, D])
        xT = sb("xT", [P, CHUNKS, W])
        hT = sb("hT", [P, M1, W])
        relu2 = sb("relu2", [P, PAIR, H2])
        p1 = sb("p1", [P, TILES])
        p2 = sb("p2", [P, TILES])
        p3 = sb("p3", [P, TILES])
        tmp = sb("tmp", [P, TILES])
        crossed = sb("crossed", [P, TILES])
        deep = sb("deep", [P, TILES])
        logit = sb("logit", [P, TILES])
        prob = sb("prob", [P, TILES])

        acc1 = pb("acc1", [P, M1, W])
        turned = pb("turned", [P, 512])
        dots = pb("dots", [P, 512])
        acc2 = pb("acc2", [P, PAIR, H2])
        BANK = 512
        M_PER_BANK = BANK // W
        BANKS1 = M1 // M_PER_BANK

        cat_in = sem("cat_in")
        num_in = sem("num_in")
        vec_in = sem("vec_in")
        bias_in = sem("bias_in")
        fold_in = sem("fold_in")
        w1_in = [sem(f"w1_in{k}") for k in range(CHUNKS)]
        w2_in = sem("w2_in")
        const_set = sem("const_set")
        ident_set = sem("ident_set")
        idx_step = sem("idx_step")
        idx_staged = sem("idx_staged")
        chunks_begun = sem("chunks_begun")
        all_idx = sem("all_idx")
        vecs_zero = sem("vecs_zero")
        vecs_turned = sem("vecs_turned")
        vecs_ready = sem("vecs_ready")
        fold_step = sem("fold_step")
        bias_part_ready = sem("bias_part_ready")
        bias_dots_done = sem("bias_dots_done")
        diag_ready = sem("diag_ready")
        head_turned = sem("head_turned")
        landed = [sem(f"landed{k}") for k in range(CHUNKS)]
        landed_last = [sem(f"landed_last{k}") for k in range(CHUNKS)]
        num_staged = sem("num_staged")
        transposed = sem("transposed")
        xT_ready = sem("xT_ready")
        l1_done = sem("l1_done")
        h_ready = sem("h_ready")
        dots_done = sem("dots_done")
        cross_step = sem("cross_step")
        l2_done = sem("l2_done")
        acc2_read = sem("acc2_read")
        logit_ready = sem("logit_ready")
        prob_ready = sem("prob_ready")
        stored = sem("stored")

        block = ctx.enter_context(nc.Block())

        LOOPS = PAIRS - 1
        CROSS_STEPS = 9

        @block.sync
        def _(sp):
            sp.dma_start(cat_sb[:, :, :], cat.rearrange("(p t) c -> p t c", p=P)).then_inc(cat_in, 16)
            sp.dma_start(wch_bc[:, :], Wc[D:D + H3, :].rearrange("n o -> o n").to_broadcast([P, H3])).then_inc(fold_in, 16)
            sp.dma_start(w3_sb[:, :, :], W3.rearrange("(c p) n -> p c n", p=P)).then_inc(fold_in, 16)
            for k in range(CHUNKS):
                sp.dma_start(w1_sb[0:width(k), k, :], W1[k * P:k * P + width(k), :]).then_inc(w1_in[k], 16)
            sp.dma_start(w2_sb[:, :, :], W2.rearrange("(c p) n -> p c n", p=P)).then_inc(w2_in, 16)
            sp.wait_ge(prob_ready, 1)
            sp.dma_start(out.rearrange("(p t) o -> p (t o)", p=P), prob[:, :]).then_inc(stored, 16)
            sp.wait_ge(stored, 16)

        @block.gpsimd
        def _(pool):
            pool.memset(ident[:, :], 0.0).then_inc(const_set, 1)
            pool.iota(table_base[:, :, :], pattern=[[0, TILES], [VOCAB, TABLES]], base=0,
                      channel_multiplier=0, allow_small_or_imprecise_dtypes=True).then_inc(const_set, 1)
            pool.memset(ones[:, :], 1.0).then_inc(const_set, 1)
            pool.wait_ge(const_set, 3)
            pool.affine_select(out=ident[:, :], in_=ident[:, :], compare_op=ALU.not_equal, fill=1.0,
                               base=0, pattern=[[-1, P]], channel_multiplier=1).then_inc(ident_set, 1)

            def gather(k, j, done):
                for t in tables(k):
                    pool.indirect_dma_start(
                        out=x[:, j, t * EMB:(t + 1) * EMB], out_offset=None, in_=rows,
                        in_offset=bass.IndirectOffsetOnAxis(ap=idx[:, j, t:t + 1], axis=0),
                    ).then_inc(done, 16)

            with pool.Fori(0, LOOPS) as g:
                for k in range(CHUNKS):
                    pool.wait_ge(idx_staged, g * CHUNKS + (k + 1))
                    pool.sem_inc(chunks_begun, 1)
                    for j in range(PAIR):
                        gather(k, j, landed[k])
            for j, done in ((0, landed), (1, landed_last)):
                for k in range(CHUNKS):
                    pool.wait_ge(idx_staged, LOOPS * CHUNKS + k + 1)
                    gather(k, j, done[k])

        @block.scalar
        def _(act):
            act.dma_start(vec_rows[0:CROSS, :], alphas).then_inc(vec_in, 16)
            act.dma_start(vec_rows[CROSS:CROSS + 1, :], Wc[0:D, :].rearrange("n o -> o n")).then_inc(vec_in, 16)
            act.dma_start(vec_rows[CROSS + 1:VECS, :], cross_bias).then_inc(vec_in, 16)
            act.dma_start(bias_rows[0:M1, :], b1.rearrange("(m p) -> m p", p=P)).then_inc(bias_in, 16)
            act.dma_start(bias_rows[M1:M1 + M2, :], b2.rearrange("(m p) -> m p", p=P)).then_inc(bias_in, 16)
            act.dma_start(bias_rows[M1 + M2:M1 + M2 + M3, :], b3.rearrange("(m p) -> m p", p=P)).then_inc(bias_in, 16)
            act.dma_start(bias_rows[M1 + M2 + M3:M1 + M2 + 2 * M3, :],
                          Wc[D:D + H3, :].rearrange("(m p) o -> m (p o)", p=P)).then_inc(bias_in, 16)
            act.dma_start(num_sb[:, :, :], num.rearrange("(p t) c -> p t c", p=P)).then_inc(num_in, 16)
            act.dma_start(b2_row[:, :], b2.rearrange("(o n) -> o n", o=1)).then_inc(fold_in, 16)
            act.dma_start(bc_bc[:, :], bc.rearrange("(o n) -> o n", o=1).to_broadcast([P, 1])).then_inc(fold_in, 16)

            act.wait_ge(head_turned, 1)
            act.activation(head_bc[:, :], acc2[:, 1, :], ACT.Copy).then_inc(acc2_read, 1)
            act.wait_ge(num_in, 16)

            def stage_numbers(g):
                act.activation(x[:, :, TABLES * EMB:D], num_sb[:, bass.ds(g * PAIR, PAIR), :], ACT.Copy).then_inc(num_staged, 1)

            def relu1(base, lo, hi):
                for m in range(M1):
                    if m % M_PER_BANK == 0:
                        act.wait_ge(l1_done, base + (m // M_PER_BANK + 1))
                    act.activation(hT[:, m, lo:hi], acc1[:, m, lo:hi], ACT.Relu,
                                   bias=bias_cols[:, m:m + 1]).then_inc(h_ready, 1)

            act.wait_ge(vecs_ready, 1)
            with act.Fori(0, LOOPS) as g:
                stage_numbers(g)
                relu1(g * BANKS1, 0, W)
            stage_numbers(LOOPS)
            for j in range(PAIR):
                relu1((LOOPS + j) * BANKS1, j * P, (j + 1) * P)
            act.wait_ge(logit_ready, 1)
            act.activation(prob[:, :], logit[:, :], ACT.Sigmoid).then_inc(prob_ready, 1)

        @block.tensor
        def _(pe):
            pe.wait_ge(ident_set, 1)
            pe.wait_ge(vec_in, 3 * 16)
            pe.wait_ge(bias_in, 4 * 16)
            for k in range(CHUNKS):
                pe.transpose(acc2[0:width(k), 0, k * VECS:(k + 1) * VECS],
                             vec_rows[:, k * P:k * P + width(k)], ident[0:VECS, 0:VECS])
            n = bias_rows.shape[0]
            pe.transpose(acc2[:, 0, CHUNKS * VECS:CHUNKS * VECS + n], bias_rows[:, :], ident[0:n, 0:n]).then_inc(vecs_turned, 1)
            pe.wait_ge(bias_part_ready, 1)
            pe.matmul(acc2[:, 0, 128:135], ones[:, :], bias_part[:, :], start=True, stop=True).then_inc(bias_dots_done, 1)
            pe.wait_ge(diag_ready, M2)
            for c in range(M2):
                mm = pe.matmul(acc2[:, 1, c * P:(c + 1) * P], ones[:, :], head_diag[:, c, :], start=True, stop=True)
            mm.then_inc(head_turned, 1)
            for k in range(CHUNKS):
                pe.wait_ge(w1_in[k], 16)
            pe.wait_ge(w2_in, 16)
            pe.wait_ge(fold_in, 4 * 16)

            def round_(tiles, done, landed_at, chunk_base, h_base, round_no, deep_base):
                lo, hi = tiles[0] * P, (tiles[-1] + 1) * P
                for k in range(CHUNKS):
                    pe.wait_ge(done[k], landed_at(k))
                    if k == CHUNKS - 1:
                        pe.wait_ge(num_staged, round_no[0])
                    for j in tiles:
                        mm = pe.transpose(turned[0:width(k), j * P:(j + 1) * P],
                                          x[:, j, k * P:k * P + width(k)], ident[:, :])
                    mm.then_inc(transposed, 1)
                    pe.wait_ge(xT_ready, chunk_base + (k + 1))
                    for m in range(M1):
                        mm = pe.matmul(acc1[:, m, lo:hi], w1_sb[0:width(k), k, m * P:(m + 1) * P],
                                       xT[0:width(k), k, lo:hi], start=(k == 0 and m % M_PER_BANK == 0),
                                       stop=(k == CHUNKS - 1), skip_group_check=True)
                        if k == CHUNKS - 1 and (m + 1) % M_PER_BANK == 0:
                            mm.then_inc(l1_done, 1)
                    if k == 0:
                        pe.wait_ge(cross_step, round_no[1] + 1)
                    for j in tiles:
                        mm = pe.matmul(dots[:, j * DOTS:(j + 1) * DOTS], xT[0:width(k), k, j * P:(j + 1) * P],
                                       vecs[0:width(k), k, 0:DOTS], start=(k == 0 and j == tiles[0]),
                                       stop=(k == CHUNKS - 1), skip_group_check=True)
                    if k == CHUNKS - 1:
                        mm.then_inc(dots_done, 1)
                for i, j in enumerate(tiles):
                    if i == 0:
                        pe.wait_ge(acc2_read, deep_base + 1)
                    pe.matmul(acc2[:, j, :], ones[0:1, :], b2_row[:, :], start=True, stop=False)
                    for m in range(M1):
                        if i == 0:
                            pe.wait_ge(h_ready, h_base + (m + 1))
                        mm = pe.matmul(acc2[:, j, :], hT[:, m, j * P:(j + 1) * P], w2_sb[:, m, :],
                                       start=False, stop=(m == M1 - 1))
                    mm.then_inc(l2_done, 1)

            pe.wait_ge(cross_step, 1)
            pe.wait_ge(acc2_read, 1)
            with pe.Fori(0, LOOPS) as g:
                round_(range(PAIR), landed, lambda k: (g + 1) * (16 * PAIR * len(tables(k))),
                       g * CHUNKS, g * M1, (g + 1, g * CROSS_STEPS), g * PAIR)
            for j, done, at in ((0, landed, LOOPS * PAIR + 1), (1, landed_last, 1)):
                r = LOOPS + j
                round_([j], done, lambda k: 16 * at * len(tables(k)), r * CHUNKS, r * M1,
                       (PAIRS, r * CROSS_STEPS), LOOPS * PAIR + j)

        @block.vector
        def _(dve):
            dve.wait_ge(cat_in, 16)
            dve.wait_ge(const_set, 3)
            steps = 0
            for t0, t1 in ((0, PAIR), (PAIR, TILES)):
                c, w, b = (a[:, t0:t1, :] for a in (clipped, wrap, table_base))
                nc.vector.tensor_scalar(c, cat_sb[:, t0:t1, :], float(VOCAB - 1), float(-VOCAB),
                                        ALU.min, ALU.max).then_inc(idx_step, 1)
                steps += 1
                dve.wait_ge(idx_step, steps)
                nc.vector.tensor_scalar(w, c, 0.0, float(VOCAB), ALU.is_lt, ALU.mult).then_inc(idx_step, 1)
                nc.vector.tensor_tensor(c, c, b, ALU.add).then_inc(idx_step, 1)
                steps += 2
                dve.wait_ge(idx_step, steps)
                if t0 == 0:
                    for k in range(CHUNKS):
                        part = slice(tables(k)[0], tables(k)[-1] + 1)
                        nc.vector.tensor_tensor(idx[:, :, part], c[:, :, part], w[:, :, part],
                                                ALU.add).then_inc(idx_staged, 1)
                else:
                    nc.vector.tensor_tensor(idx_all[:, t0:t1, :], c, w, ALU.add).then_inc(all_idx, 1)

            nc.vector.memset(vecs[:, :, :], 0.0).then_inc(vecs_zero, 1)
            nc.vector.memset(bias_prod[:, :, :], 0.0).then_inc(vecs_zero, 1)
            dve.wait_ge(vecs_zero, 2)
            dve.wait_ge(vecs_turned, 1)
            turned_vecs = acc2[:, 0, 0:CHUNKS * VECS].rearrange("p (k v) -> p k v", v=VECS)
            nc.vector.tensor_copy(vecs[:, 0:FULL, :], turned_vecs[:, 0:FULL, :]).then_inc(fold_step, 1)
            nc.vector.tensor_copy(vecs[0:LAST, FULL, :], turned_vecs[0:LAST, FULL, :]).then_inc(fold_step, 1)
            nc.vector.tensor_copy(bias_cols[:, :], acc2[:, 0, CHUNKS * VECS:CHUNKS * VECS + bias_rows.shape[0]]).then_inc(fold_step, 1)
            dve.wait_ge(fold_step, 3)
            for i, (u, v) in enumerate(BIAS_DOTS):
                nc.vector.tensor_tensor(bias_prod[:, i, :], vecs[:, :, u], vecs[:, :, v], ALU.mult).then_inc(fold_step, 1)
            nc.vector.tensor_tensor(bias_prod[:, B3WC, 0:M3], bias_cols[:, M1 + M2:M1 + M2 + M3],
                                    bias_cols[:, M1 + M2 + M3:M1 + M2 + 2 * M3], ALU.mult).then_inc(fold_step, 1)
            dve.wait_ge(fold_step, 10)
            nc.vector.tensor_reduce(bias_part[:, :], bias_prod[:, :, :], AX.X, ALU.add).then_inc(bias_part_ready, 1)
            dve.wait_ge(fold_in, 4 * 16)
            nc.vector.tensor_tensor(w3_prod[:, :, :], w3_sb[:, :, :],
                                    wch_bc[:, None, :].to_broadcast([P, M2, H3]), ALU.mult).then_inc(fold_step, 1)
            dve.wait_ge(fold_step, 11)
            nc.vector.tensor_reduce(head[:, :], w3_prod[:, :, :], AX.X, ALU.add).then_inc(fold_step, 1)
            dve.wait_ge(fold_step, 12)
            dve.wait_ge(ident_set, 1)
            for c in range(M2):
                nc.vector.tensor_scalar(head_diag[:, c, :], ident[:, :], head[:, c:c + 1], None,
                                        ALU.mult).then_inc(diag_ready, 1)
            dve.wait_ge(bias_dots_done, 1)
            nc.vector.tensor_copy(cst[:, 0:7], acc2[:, 0, 128:135]).then_inc(fold_step, 1)
            dve.wait_ge(fold_step, 13)
            nc.vector.scalar_tensor_tensor(cst[:, 7:8], cst[:, GAMMA2:GAMMA2 + 1], cst[:, B3WC:B3WC + 1],
                                           bc_bc[:, :], ALU.add, ALU.add).then_inc(cross_step, 1)
            nc.vector.tensor_copy(tmp[:, 0:1], bias_cols[:, 0:1]).then_inc(vecs_ready, 1)
            dve.wait_ge(all_idx, 1)
            dve.wait_ge(cross_step, 1)
            dve.wait_ge(vecs_ready, 1)
            dve.wait_ge(acc2_read, 1)

            def const(i):
                return cst[:, i:i + 1]

            def round_(tiles, chunk_base, t_at, step_base, round_no, l2_base, next_pair):
                lo, hi = tiles[0] * P, (tiles[-1] + 1) * P
                for k in range(CHUNKS):
                    dve.wait_ge(transposed, chunk_base + (k + 1))
                    nc.vector.tensor_copy(xT[0:width(k), k, lo:hi], turned[0:width(k), lo:hi]).then_inc(xT_ready, 1)
                    if next_pair is not None:
                        part = slice(tables(k)[0], tables(k)[-1] + 1)
                        nc.vector.tensor_copy(idx[:, :, part], idx_all[:, bass.ds(next_pair * PAIR, PAIR), part]).then_inc(idx_staged, 1)
                cols = bass.ds(t_at, len(tiles))
                dot = dots[:, 0:PAIR * DOTS].rearrange("p (j d) -> p j d", d=DOTS)[:, tiles[0]:tiles[-1] + 1, :]
                q1, q2, q3, q = (a[:, cols] for a in (p1, p2, p3, tmp))
                dve.wait_ge(dots_done, round_no)
                nc.vector.tensor_scalar(q1, dot[:, :, 0], 1.0, None, ALU.add).then_inc(cross_step, 1)
                dve.wait_ge(cross_step, step_base + 2)
                nc.vector.tensor_tensor(q2, dot[:, :, 1], q1, ALU.mult).then_inc(cross_step, 1)
                nc.vector.tensor_tensor(q3, dot[:, :, 2], q1, ALU.mult).then_inc(cross_step, 1)
                nc.vector.tensor_tensor(q, dot[:, :, 3], q1, ALU.mult).then_inc(cross_step, 1)
                dve.wait_ge(cross_step, step_base + 5)
                nc.vector.tensor_scalar(q2, q2, const(BETA01), 1.0, ALU.add, ALU.add).then_inc(cross_step, 1)
                dve.wait_ge(cross_step, step_base + 6)
                nc.vector.scalar_tensor_tensor(q3, q3, const(BETA02), q2, ALU.add, ALU.mult).then_inc(cross_step, 1)
                nc.vector.scalar_tensor_tensor(q, q, const(GAMMA0), q2, ALU.add, ALU.mult).then_inc(cross_step, 1)
                dve.wait_ge(cross_step, step_base + 8)
                nc.vector.tensor_scalar(q3, q3, const(BETA12), 1.0, ALU.add, ALU.add).then_inc(cross_step, 1)
                dve.wait_ge(cross_step, step_base + 9)
                nc.vector.scalar_tensor_tensor(crossed[:, cols], q, const(GAMMA1), q3, ALU.add, ALU.mult).then_inc(cross_step, 1)
                for i, j in enumerate(tiles):
                    dve.wait_ge(l2_done, l2_base + (i + 1))
                    nc.vector.scalar_tensor_tensor(relu2[:, j, :], acc2[:, j, :], 0.0, head_bc[:, :], ALU.max, ALU.mult,
                                                   accum_out=deep[:, bass.ds(t_at + i, 1)]).then_inc(acc2_read, 1)

            with dve.Fori(0, LOOPS) as g:
                round_(range(PAIR), g * CHUNKS, g * PAIR, g * CROSS_STEPS, g + 1, g * PAIR, g + 1)
            for j in range(PAIR):
                r = LOOPS + j
                round_([j], r * CHUNKS, LOOPS * PAIR + j, r * CROSS_STEPS, r + 1, LOOPS * PAIR + j, None)
            dve.wait_ge(acc2_read, TILES + 1)
            dve.wait_ge(cross_step, (LOOPS + PAIR) * CROSS_STEPS + 1)
            nc.vector.scalar_tensor_tensor(logit[:, :], crossed[:, :], const(7), deep[:, :],
                                           ALU.add, ALU.add).then_inc(logit_ready, 1)


_PREFIX = "L0_rec_"
_INS = ["r_categorical_input"] + [_PREFIX + n for n in (
    "numerical_input", "emb_tables", "alphas", "cross_bias", "W1", "b1", "W2", "b2", "W3", "b3", "Wc", "bc")]


def kernel(**inputs):
    import numpy as _np
    import concourse.bacc as _bacc
    from concourse import mybir as _mybir
    from concourse.bass_utils import run_bass_kernel_spmd as _run

    nc = _bacc.Bacc("TRN2", target_bir_lowering=False, num_devices=1)
    arrays, args = {}, []
    for name in _INS:
        a = _np.ascontiguousarray(inputs[name])
        arrays[f"in_{name}_dram"] = a
        args.append(nc.dram_tensor(f"in_{name}_dram", a.shape, _mybir.dt.from_np(a.dtype), kind="ExternalInput").ap())
    shape = (inputs["r_categorical_input"].shape[0], inputs[_PREFIX + "Wc"].shape[1])
    args.append(nc.dram_tensor("out_dram", shape, _mybir.dt.float32, kind="ExternalOutput").ap())
    deep_cross_kernel(nc, *args)
    r = _run(nc, [arrays], core_ids=[0])
    return r.results[0]["out_dram"]
```

```python
import concourse.bass as bass
from concourse import mybir
from contextlib import ExitStack


def deep_cross_kernel(nc, cat, num, emb, alphas, cross_bias, W1, b1, W2, b2, W3, b3, Wc, bc, out):
    fp32, bf16, i32 = mybir.dt.float32, mybir.dt.bfloat16, mybir.dt.int32
    ALU = mybir.AluOpType
    ACT = mybir.ActivationFunctionType
    AX = mybir.AxisListType

    P = 128
    B, TABLES = cat.shape
    _, VOCAB, EMB = emb.shape
    NUMS = num.shape[1]
    D, H1 = W1.shape
    H2 = W2.shape[1]
    H3 = W3.shape[1]
    CROSS = alphas.shape[0]
    TILES = B // P
    PER_CHUNK = P // EMB
    CHUNKS = (D + P - 1) // P
    FULL = D // P
    LAST = D - FULL * P
    M1, M2, M3 = H1 // P, H2 // P, H3 // P
    PAIR = 2
    PAIRS = TILES // PAIR
    W = PAIR * P
    VECS = 2 * CROSS + 1
    DOTS = CROSS + 1
    BETA01, BETA02, BETA12, GAMMA0, GAMMA1, GAMMA2, B3WC = range(7)
    BIAS_DOTS = ((CROSS + 1, 1), (CROSS + 1, 2), (CROSS + 2, 2), (CROSS + 1, CROSS), (CROSS + 2, CROSS), (CROSS + 3, CROSS))

    def tables(k):
        return range(k * PER_CHUNK, min((k + 1) * PER_CHUNK, TABLES))

    def width(k):
        return P if k < FULL else LAST

    rows = emb.rearrange("t v e -> (t v) e")

    ctx = ExitStack()
    with ctx:
        def sb(name, shape, dt=fp32):
            return ctx.enter_context(nc.sbuf_tensor(name, shape, dt))

        def pb(name, shape):
            return ctx.enter_context(nc.psum_tensor(name, shape, fp32))

        def sem(name):
            return ctx.enter_context(nc.semaphore(name))

        cat_sb = sb("cat_sb", [P, TILES, TABLES], i32)
        num_sb = sb("num_sb", [P, TILES, NUMS])
        vec_rows = sb("vec_rows", [VECS, D])
        bias_rows = sb("bias_rows", [M1 + M2 + 2 * M3, P])
        w1_sb = sb("w1_sb", [P, CHUNKS, H1])
        w2_sb = sb("w2_sb", [P, M1, H2])
        w3_sb = sb("w3_sb", [P, M2, H3])
        wch_bc = sb("wch_bc", [P, H3])
        THREE = 96
        b2_rows = sb("b2_rows", [THREE, H2])
        b2_rest = sb("b2_rest", [THREE, H2])
        b2_rest2 = sb("b2_rest2", [THREE, H2])
        b2_cut = [sb(f"b2_cut{i}", [THREE, H2], bf16) for i in range(3)]
        b2_parts = sb("b2_parts", [THREE, H2], bf16)
        ones_bf = sb("ones_bf", [THREE, P], bf16)
        bc_bc = sb("bc_bc", [P, 1])
        ident = sb("ident", [P, P])
        ones = sb("ones", [P, P])
        table_base = sb("table_base", [P, TILES, TABLES])
        vecs = sb("vecs", [P, CHUNKS, VECS])
        bias_cols = sb("bias_cols", [P, M1 + M2 + 2 * M3])
        bias_prod = sb("bias_prod", [P, 7, CHUNKS])
        bias_part = sb("bias_part", [P, 7])
        cst = sb("cst", [P, 8])
        w3_prod = sb("w3_prod", [P, M2, H3])
        head = sb("head", [P, M2])
        head_diag = sb("head_diag", [P, M2, P])
        head_bc = sb("head_bc", [P, H2])
        clipped = sb("clipped", [P, TILES, TABLES])
        wrap = sb("wrap", [P, TILES, TABLES])
        idx_all = sb("idx_all", [P, TILES, TABLES], i32)
        idx = sb("idx", [P, PAIR, TABLES], i32)
        x = sb("x", [P, PAIR, D])
        xT = sb("xT", [P, CHUNKS, W])
        hT = sb("hT", [P, M1, W])
        relu2 = sb("relu2", [P, PAIR, H2])
        dots_sb = sb("dots_sb", [P, TILES, DOTS])
        p1 = sb("p1", [P, TILES])
        p2 = sb("p2", [P, TILES])
        p3 = sb("p3", [P, TILES])
        tmp = sb("tmp", [P, TILES])
        crossed = sb("crossed", [P, TILES])
        deep = sb("deep", [P, TILES])
        logit = sb("logit", [P, TILES])
        prob = sb("prob", [P, TILES])

        acc1 = pb("acc1", [P, M1, W])
        turned = pb("turned", [P, 512])
        dots = pb("dots", [P, 512])
        acc2 = pb("acc2", [P, PAIR, H2])
        BANK = 512
        M_PER_BANK = BANK // W
        BANKS1 = M1 // M_PER_BANK

        cat_in = sem("cat_in")
        num_in = sem("num_in")
        vec_in = sem("vec_in")
        bias_in = sem("bias_in")
        fold_in = sem("fold_in")
        w1_in = [sem(f"w1_in{k}") for k in range(CHUNKS)]
        w2_in = sem("w2_in")
        const_set = sem("const_set")
        ident_set = sem("ident_set")
        idx_step = sem("idx_step")
        idx_staged = sem("idx_staged")
        chunks_begun = sem("chunks_begun")
        all_idx = sem("all_idx")
        vecs_zero = sem("vecs_zero")
        vecs_turned = sem("vecs_turned")
        vecs_ready = sem("vecs_ready")
        fold_step = sem("fold_step")
        bias_part_ready = sem("bias_part_ready")
        bias_dots_done = sem("bias_dots_done")
        diag_ready = sem("diag_ready")
        head_turned = sem("head_turned")
        landed = [sem(f"landed{k}") for k in range(CHUNKS)]
        landed_last = [sem(f"landed_last{k}") for k in range(CHUNKS)]
        num_staged = sem("num_staged")
        transposed = sem("transposed")
        xT_ready = sem("xT_ready")
        l1_done = sem("l1_done")
        h_ready = sem("h_ready")
        dots_done = sem("dots_done")
        dots_read = sem("dots_read")
        cst_ready = sem("cst_ready")
        b2_step = sem("b2_step")
        b2_ready = sem("b2_ready")
        cross_step = sem("cross_step")
        l2_done = sem("l2_done")
        acc2_read = sem("acc2_read")
        logit_ready = sem("logit_ready")
        prob_ready = sem("prob_ready")
        stored = sem("stored")

        block = ctx.enter_context(nc.Block())

        LOOPS = PAIRS - 1

        @block.sync
        def _(sp):
            sp.dma_start(cat_sb[:, :, :], cat.rearrange("(p t) c -> p t c", p=P)).then_inc(cat_in, 16)
            sp.dma_start(wch_bc[:, :], Wc[D:D + H3, :].rearrange("n o -> o n").to_broadcast([P, H3])).then_inc(fold_in, 16)
            sp.dma_start(w3_sb[:, :, :], W3.rearrange("(c p) n -> p c n", p=P)).then_inc(fold_in, 16)
            for k in range(CHUNKS):
                sp.dma_start(w1_sb[0:width(k), k, :], W1[k * P:k * P + width(k), :]).then_inc(w1_in[k], 16)
            sp.dma_start(w2_sb[:, :, :], W2.rearrange("(c p) n -> p c n", p=P)).then_inc(w2_in, 16)
            sp.wait_ge(prob_ready, 1)
            sp.dma_start(out.rearrange("(p t) o -> p (t o)", p=P), prob[:, :]).then_inc(stored, 16)
            sp.wait_ge(stored, 16)

        @block.gpsimd
        def _(pool):
            pool.memset(ident[:, :], 0.0).then_inc(const_set, 1)
            pool.iota(table_base[:, :, :], pattern=[[0, TILES], [VOCAB, TABLES]], base=0,
                      channel_multiplier=0, allow_small_or_imprecise_dtypes=True).then_inc(const_set, 1)
            pool.memset(ones[:, :], 1.0).then_inc(const_set, 1)
            pool.wait_ge(const_set, 3)
            pool.affine_select(out=ident[:, :], in_=ident[:, :], compare_op=ALU.not_equal, fill=1.0,
                               base=0, pattern=[[-1, P]], channel_multiplier=1).then_inc(ident_set, 1)

            def gather(k, j, done):
                for t in tables(k):
                    pool.indirect_dma_start(
                        out=x[:, j, t * EMB:(t + 1) * EMB], out_offset=None, in_=rows,
                        in_offset=bass.IndirectOffsetOnAxis(ap=idx[:, j, t:t + 1], axis=0),
                    ).then_inc(done, 16)

            with pool.Fori(0, LOOPS) as g:
                for k in range(CHUNKS):
                    pool.wait_ge(idx_staged, g * CHUNKS + (k + 1))
                    pool.sem_inc(chunks_begun, 1)
                    for j in range(PAIR):
                        gather(k, j, landed[k])
            for j, done in ((0, landed), (1, landed_last)):
                for k in range(CHUNKS):
                    pool.wait_ge(idx_staged, LOOPS * CHUNKS + k + 1)
                    gather(k, j, done[k])

        @block.scalar
        def _(act):
            act.dma_start(vec_rows[0:CROSS, :], alphas).then_inc(vec_in, 16)
            act.dma_start(vec_rows[CROSS:CROSS + 1, :], Wc[0:D, :].rearrange("n o -> o n")).then_inc(vec_in, 16)
            act.dma_start(vec_rows[CROSS + 1:VECS, :], cross_bias).then_inc(vec_in, 16)
            act.dma_start(bias_rows[0:M1, :], b1.rearrange("(m p) -> m p", p=P)).then_inc(bias_in, 16)
            act.dma_start(bias_rows[M1:M1 + M2, :], b2.rearrange("(m p) -> m p", p=P)).then_inc(bias_in, 16)
            act.dma_start(bias_rows[M1 + M2:M1 + M2 + M3, :], b3.rearrange("(m p) -> m p", p=P)).then_inc(bias_in, 16)
            act.dma_start(bias_rows[M1 + M2 + M3:M1 + M2 + 2 * M3, :],
                          Wc[D:D + H3, :].rearrange("(m p) o -> m (p o)", p=P)).then_inc(bias_in, 16)
            act.dma_start(num_sb[:, :, :], num.rearrange("(p t) c -> p t c", p=P)).then_inc(num_in, 16)
            act.dma_start(b2_rows[:, :], b2.rearrange("(o n) -> o n", o=1).to_broadcast([THREE, H2])).then_inc(fold_in, 16)
            act.dma_start(bc_bc[:, :], bc.rearrange("(o n) -> o n", o=1).to_broadcast([P, 1])).then_inc(fold_in, 16)

            act.wait_ge(head_turned, 1)
            act.activation(head_bc[:, :], acc2[:, 1, :], ACT.Copy).then_inc(acc2_read, 1)
            act.wait_ge(num_in, 16)

            def stage_numbers(g):
                act.activation(x[:, :, TABLES * EMB:D], num_sb[:, bass.ds(g * PAIR, PAIR), :], ACT.Copy).then_inc(num_staged, 1)

            def relu1(base, lo, hi):
                for m in range(M1):
                    if m % M_PER_BANK == 0:
                        act.wait_ge(l1_done, base + (m // M_PER_BANK + 1))
                    act.activation(hT[:, m, lo:hi], acc1[:, m, lo:hi], ACT.Relu,
                                   bias=bias_cols[:, m:m + 1]).then_inc(h_ready, 1)

            act.wait_ge(vecs_ready, 1)
            with act.Fori(0, LOOPS) as g:
                stage_numbers(g)
                relu1(g * BANKS1, 0, W)
            stage_numbers(LOOPS)
            for j in range(PAIR):
                relu1((LOOPS + j) * BANKS1, j * P, (j + 1) * P)
            act.wait_ge(logit_ready, 1)
            act.activation(prob[:, :], logit[:, :], ACT.Sigmoid).then_inc(prob_ready, 1)

        @block.tensor
        def _(pe):
            pe.wait_ge(ident_set, 1)
            pe.wait_ge(vec_in, 3 * 16)
            pe.wait_ge(bias_in, 4 * 16)
            for k in range(CHUNKS):
                pe.transpose(acc2[0:width(k), 0, k * VECS:(k + 1) * VECS],
                             vec_rows[:, k * P:k * P + width(k)], ident[0:VECS, 0:VECS])
            n = bias_rows.shape[0]
            pe.transpose(acc2[:, 0, CHUNKS * VECS:CHUNKS * VECS + n], bias_rows[:, :], ident[0:n, 0:n]).then_inc(vecs_turned, 1)
            pe.wait_ge(bias_part_ready, 1)
            pe.matmul(acc2[:, 0, 128:135], ones[:, :], bias_part[:, :], start=True, stop=True).then_inc(bias_dots_done, 1)
            pe.wait_ge(diag_ready, M2)
            for c in range(M2):
                mm = pe.matmul(acc2[:, 1, c * P:(c + 1) * P], ones[:, :], head_diag[:, c, :], start=True, stop=True)
            mm.then_inc(head_turned, 1)
            for k in range(CHUNKS):
                pe.wait_ge(w1_in[k], 16)
            pe.wait_ge(w2_in, 16)
            pe.wait_ge(b2_ready, 3)

            def layer1(tiles, done, landed_at, r, numbers, fillers, first=False):
                lo, hi = tiles[0] * P, (tiles[-1] + 1) * P
                for k in range(CHUNKS):
                    pe.wait_ge(done[k], landed_at(k))
                    if k == CHUNKS - 1:
                        pe.wait_ge(num_staged, numbers)
                    for j in tiles:
                        mm = pe.transpose(turned[0:width(k), j * P:(j + 1) * P],
                                          x[:, j, k * P:k * P + width(k)], ident[:, :])
                    mm.then_inc(transposed, 1)
                    for filler in fillers[k]:
                        filler()
                    pe.wait_ge(xT_ready, r * CHUNKS + (k + 1))
                    for m in range(M1):
                        if k == 0 and m % M_PER_BANK == 0 and not first:
                            pe.wait_ge(h_ready, (r - 1) * M1 + (m + M_PER_BANK))
                        mm = pe.matmul(acc1[:, m, lo:hi], w1_sb[0:width(k), k, m * P:(m + 1) * P],
                                       xT[0:width(k), k, lo:hi], start=(k == 0 and m % M_PER_BANK == 0),
                                       stop=(k == CHUNKS - 1), skip_group_check=True)
                        if k == CHUNKS - 1 and (m + 1) % M_PER_BANK == 0:
                            mm.then_inc(l1_done, 1)
                    if k == 0 and not first:
                        pe.wait_ge(dots_read, r)
                    for j in tiles:
                        mm = pe.matmul(dots[:, j * DOTS:(j + 1) * DOTS], xT[0:width(k), k, j * P:(j + 1) * P],
                                       vecs[0:width(k), k, 0:DOTS], start=(k == 0 and j == tiles[0]),
                                       stop=(k == CHUNKS - 1), skip_group_check=True)
                    if k == CHUNKS - 1:
                        mm.then_inc(dots_done, 1)

            def layer2_bias(j, read):
                pe.wait_ge(acc2_read, read)
                pe.matmul(acc2[:, j, :], ones_bf[:, :], b2_parts[:, :], start=True, stop=False)

            def layer2_block(j, m, r):
                pe.wait_ge(h_ready, r * M1 + (m + 1))
                mm = pe.matmul(acc2[:, j, :], hT[:, m, j * P:(j + 1) * P], w2_sb[:, m, :],
                               start=False, stop=(m == M1 - 1))
                if m == M1 - 1:
                    mm.then_inc(l2_done, 1)

            def layer2(tiles, r, reads):
                return [part for i, j in enumerate(tiles) for part in
                        [lambda j=j, i=i: layer2_bias(j, reads[i])]
                        + [lambda j=j, m=m: layer2_block(j, m, r) for m in range(M1)]]

            def spread(parts):
                n = CHUNKS - 1
                cut = [-(-len(parts) * k // n) for k in range(n + 1)]
                return [parts[cut[k]:cut[k + 1]] for k in range(n)] + [[]]

            def pair_landed(g):
                return lambda k: (g + 1) * (16 * PAIR * len(tables(k)))

            both = range(PAIR)
            pe.wait_ge(cst_ready, 1)
            pe.wait_ge(acc2_read, 1)
            layer1(both, landed, pair_landed(0), 0, 1, [[]] * CHUNKS, first=True)
            with pe.Fori(1, LOOPS) as g:
                layer1(both, landed, pair_landed(g), g, g + 1,
                       spread(layer2(both, g - 1, [(g - 1) * PAIR + 1] * PAIR)))
            layer1([0], landed, lambda k: 16 * (LOOPS * PAIR + 1) * len(tables(k)), LOOPS, PAIRS,
                   spread(layer2(both, LOOPS - 1, [(LOOPS - 1) * PAIR + 1] * PAIR)))
            second = layer2([1], LOOPS + 1, [LOOPS * PAIR + 1])
            layer1([1], landed_last, lambda k: 16 * len(tables(k)), LOOPS + 1, PAIRS,
                   spread(layer2([0], LOOPS, [LOOPS * PAIR + 1]) + second[:1]))
            for part in second[1:]:
                part()

        @block.vector
        def _(dve):
            dve.wait_ge(cat_in, 16)
            dve.wait_ge(const_set, 3)
            steps = 0
            for t0, t1 in ((0, PAIR), (PAIR, TILES)):
                c, w, b = (a[:, t0:t1, :] for a in (clipped, wrap, table_base))
                nc.vector.tensor_scalar(c, cat_sb[:, t0:t1, :], float(VOCAB - 1), float(-VOCAB),
                                        ALU.min, ALU.max).then_inc(idx_step, 1)
                steps += 1
                dve.wait_ge(idx_step, steps)
                nc.vector.tensor_scalar(w, c, 0.0, float(VOCAB), ALU.is_lt, ALU.mult).then_inc(idx_step, 1)
                nc.vector.tensor_tensor(c, c, b, ALU.add).then_inc(idx_step, 1)
                steps += 2
                dve.wait_ge(idx_step, steps)
                if t0 == 0:
                    for k in range(CHUNKS):
                        part = slice(tables(k)[0], tables(k)[-1] + 1)
                        nc.vector.tensor_tensor(idx[:, :, part], c[:, :, part], w[:, :, part],
                                                ALU.add).then_inc(idx_staged, 1)
                else:
                    nc.vector.tensor_tensor(idx_all[:, t0:t1, :], c, w, ALU.add).then_inc(all_idx, 1)

            nc.vector.memset(vecs[:, :, :], 0.0).then_inc(vecs_zero, 1)
            nc.vector.memset(bias_prod[:, :, :], 0.0).then_inc(vecs_zero, 1)
            dve.wait_ge(vecs_zero, 2)
            dve.wait_ge(vecs_turned, 1)
            turned_vecs = acc2[:, 0, 0:CHUNKS * VECS].rearrange("p (k v) -> p k v", v=VECS)
            nc.vector.tensor_copy(vecs[:, 0:FULL, :], turned_vecs[:, 0:FULL, :]).then_inc(fold_step, 1)
            nc.vector.tensor_copy(vecs[0:LAST, FULL, :], turned_vecs[0:LAST, FULL, :]).then_inc(fold_step, 1)
            nc.vector.tensor_copy(bias_cols[:, :], acc2[:, 0, CHUNKS * VECS:CHUNKS * VECS + bias_rows.shape[0]]).then_inc(fold_step, 1)
            dve.wait_ge(fold_step, 3)
            for i, (u, v) in enumerate(BIAS_DOTS):
                nc.vector.tensor_tensor(bias_prod[:, i, :], vecs[:, :, u], vecs[:, :, v], ALU.mult).then_inc(fold_step, 1)
            nc.vector.tensor_tensor(bias_prod[:, B3WC, 0:M3], bias_cols[:, M1 + M2:M1 + M2 + M3],
                                    bias_cols[:, M1 + M2 + M3:M1 + M2 + 2 * M3], ALU.mult).then_inc(fold_step, 1)
            dve.wait_ge(fold_step, 10)
            nc.vector.tensor_reduce(bias_part[:, :], bias_prod[:, :, :], AX.X, ALU.add).then_inc(bias_part_ready, 1)
            dve.wait_ge(fold_in, 4 * 16)
            nc.vector.tensor_tensor(w3_prod[:, :, :], w3_sb[:, :, :],
                                    wch_bc[:, None, :].to_broadcast([P, M2, H3]), ALU.mult).then_inc(fold_step, 1)
            dve.wait_ge(fold_step, 11)
            nc.vector.tensor_reduce(head[:, :], w3_prod[:, :, :], AX.X, ALU.add).then_inc(fold_step, 1)
            dve.wait_ge(fold_step, 12)
            dve.wait_ge(ident_set, 1)
            for c in range(M2):
                nc.vector.tensor_scalar(head_diag[:, c, :], ident[:, :], head[:, c:c + 1], None,
                                        ALU.mult).then_inc(diag_ready, 1)
            dve.wait_ge(bias_dots_done, 1)
            nc.vector.tensor_copy(cst[:, 0:7], acc2[:, 0, 128:135]).then_inc(fold_step, 1)
            dve.wait_ge(fold_step, 13)
            nc.vector.scalar_tensor_tensor(cst[:, 7:8], cst[:, GAMMA2:GAMMA2 + 1], cst[:, B3WC:B3WC + 1],
                                           bc_bc[:, :], ALU.add, ALU.add).then_inc(cst_ready, 1)
            nc.vector.tensor_copy(tmp[:, 0:1], bias_cols[:, 0:1]).then_inc(vecs_ready, 1)
            nc.vector.memset(b2_parts[:, :], 0.0).then_inc(b2_step, 1)
            nc.vector.memset(ones_bf[:, :], 1.0).then_inc(b2_step, 1)
            nc.vector.tensor_copy(b2_cut[0][:, :], b2_rows[:, :]).then_inc(b2_step, 1)
            dve.wait_ge(b2_step, 3)
            nc.vector.tensor_tensor(b2_rest[:, :], b2_rows[:, :], b2_cut[0][:, :], ALU.subtract).then_inc(b2_step, 1)
            dve.wait_ge(b2_step, 4)
            nc.vector.tensor_copy(b2_cut[1][:, :], b2_rest[:, :]).then_inc(b2_step, 1)
            dve.wait_ge(b2_step, 5)
            nc.vector.tensor_tensor(b2_rest2[:, :], b2_rest[:, :], b2_cut[1][:, :], ALU.subtract).then_inc(b2_step, 1)
            dve.wait_ge(b2_step, 6)
            nc.vector.tensor_copy(b2_cut[2][:, :], b2_rest2[:, :]).then_inc(b2_step, 1)
            dve.wait_ge(b2_step, 7)
            for i in range(3):
                nc.vector.tensor_copy(b2_parts[32 * i:32 * i + 1, :], b2_cut[i][32 * i:32 * i + 1, :]).then_inc(b2_ready, 1)
            dve.wait_ge(all_idx, 1)
            dve.wait_ge(cst_ready, 1)
            dve.wait_ge(vecs_ready, 1)
            dve.wait_ge(acc2_read, 1)

            def const(i):
                return cst[:, i:i + 1]

            def deep_share(j, t):
                dve.wait_ge(l2_done, t + 1)
                nc.vector.scalar_tensor_tensor(relu2[:, j, :], acc2[:, j, :], 0.0, head_bc[:, :], ALU.max, ALU.mult,
                                               accum_out=deep[:, bass.ds(t, 1)]).then_inc(acc2_read, 1)

            def follow(tiles, r, t_at, next_pair, shares):
                lo, hi = tiles[0] * P, (tiles[-1] + 1) * P
                for k in range(CHUNKS):
                    dve.wait_ge(transposed, r * CHUNKS + (k + 1))
                    nc.vector.tensor_copy(xT[0:width(k), k, lo:hi], turned[0:width(k), lo:hi]).then_inc(xT_ready, 1)
                    if next_pair is not None:
                        part = slice(tables(k)[0], tables(k)[-1] + 1)
                        nc.vector.tensor_copy(idx[:, :, part], idx_all[:, bass.ds(next_pair * PAIR, PAIR), part]).then_inc(idx_staged, 1)
                    if k in shares:
                        deep_share(*shares[k])
                dve.wait_ge(dots_done, r + 1)
                nc.vector.tensor_copy(dots_sb[:, bass.ds(t_at, len(tiles)), :],
                                      dots[:, 0:PAIR * DOTS].rearrange("p (j d) -> p j d", d=DOTS)[:, tiles[0]:tiles[-1] + 1, :],
                                      ).then_inc(dots_read, 1)

            def pair_shares(pair):
                return {CHUNKS // 2: (0, pair * PAIR), CHUNKS - 1: (1, pair * PAIR + 1)}

            both = range(PAIR)
            follow(both, 0, 0, 1, {})
            with dve.Fori(1, LOOPS) as g:
                follow(both, g, g * PAIR, g + 1, pair_shares(g - 1))
            follow([0], LOOPS, LOOPS * PAIR, None, pair_shares(LOOPS - 1))
            follow([1], LOOPS + 1, LOOPS * PAIR + 1, None, {CHUNKS - 1: (0, LOOPS * PAIR)})

            dot = [dots_sb[:, :, d] for d in range(DOTS)]
            q1, q2, q3, q = (a[:, :] for a in (p1, p2, p3, tmp))
            dve.wait_ge(dots_read, LOOPS + PAIR)
            nc.vector.tensor_scalar(q1, dot[0], 1.0, None, ALU.add).then_inc(cross_step, 1)
            dve.wait_ge(cross_step, 1)
            nc.vector.tensor_tensor(q2, dot[1], q1, ALU.mult).then_inc(cross_step, 1)
            nc.vector.tensor_tensor(q3, dot[2], q1, ALU.mult).then_inc(cross_step, 1)
            nc.vector.tensor_tensor(q, dot[3], q1, ALU.mult).then_inc(cross_step, 1)
            dve.wait_ge(cross_step, 4)
            nc.vector.tensor_scalar(q2, q2, const(BETA01), 1.0, ALU.add, ALU.add).then_inc(cross_step, 1)
            dve.wait_ge(cross_step, 5)
            nc.vector.scalar_tensor_tensor(q3, q3, const(BETA02), q2, ALU.add, ALU.mult).then_inc(cross_step, 1)
            nc.vector.scalar_tensor_tensor(q, q, const(GAMMA0), q2, ALU.add, ALU.mult).then_inc(cross_step, 1)
            dve.wait_ge(cross_step, 7)
            nc.vector.tensor_scalar(q3, q3, const(BETA12), 1.0, ALU.add, ALU.add).then_inc(cross_step, 1)
            dve.wait_ge(cross_step, 8)
            nc.vector.scalar_tensor_tensor(crossed[:, :], q, const(GAMMA1), q3, ALU.add, ALU.mult).then_inc(cross_step, 1)
            deep_share(1, LOOPS * PAIR + 1)
            dve.wait_ge(acc2_read, TILES + 1)
            dve.wait_ge(cross_step, 9)
            nc.vector.scalar_tensor_tensor(logit[:, :], crossed[:, :], const(7), deep[:, :],
                                           ALU.add, ALU.add).then_inc(logit_ready, 1)


_PREFIX = "L0_rec_"
_INS = ["r_categorical_input"] + [_PREFIX + n for n in (
    "numerical_input", "emb_tables", "alphas", "cross_bias", "W1", "b1", "W2", "b2", "W3", "b3", "Wc", "bc")]


def kernel(**inputs):
    import numpy as _np
    import concourse.bacc as _bacc
    from concourse import mybir as _mybir
    from concourse.bass_utils import run_bass_kernel_spmd as _run

    nc = _bacc.Bacc("TRN2", target_bir_lowering=False, num_devices=1)
    arrays, args = {}, []
    for name in _INS:
        a = _np.ascontiguousarray(inputs[name])
        arrays[f"in_{name}_dram"] = a
        args.append(nc.dram_tensor(f"in_{name}_dram", a.shape, _mybir.dt.from_np(a.dtype), kind="ExternalInput").ap())
    shape = (inputs["r_categorical_input"].shape[0], inputs[_PREFIX + "Wc"].shape[1])
    args.append(nc.dram_tensor("out_dram", shape, _mybir.dt.float32, kind="ExternalOutput").ap())
    deep_cross_kernel(nc, *args)
    r = _run(nc, [arrays], core_ids=[0])
    return r.results[0]["out_dram"]
```

```python
import concourse.bass as bass
from concourse import mybir
from contextlib import ExitStack


def deep_cross_kernel(nc, cat, num, emb, alphas, cross_bias, W1, b1, W2, b2, W3, b3, Wc, bc, out):
    fp32, bf16, i32 = mybir.dt.float32, mybir.dt.bfloat16, mybir.dt.int32
    ALU = mybir.AluOpType
    ACT = mybir.ActivationFunctionType
    AX = mybir.AxisListType

    P = 128
    B, TABLES = cat.shape
    _, VOCAB, EMB = emb.shape
    NUMS = num.shape[1]
    D, H1 = W1.shape
    H2 = W2.shape[1]
    H3 = W3.shape[1]
    CROSS = alphas.shape[0]
    TILES = B // P
    PER_CHUNK = P // EMB
    CHUNKS = (D + P - 1) // P
    FULL = D // P
    LAST = D - FULL * P
    M1, M2, M3 = H1 // P, H2 // P, H3 // P
    PAIR = 2
    PAIRS = TILES // PAIR
    W = PAIR * P
    VECS = 2 * CROSS + 1
    DOTS = CROSS + 1
    BETA01, BETA02, BETA12, GAMMA0, GAMMA1, GAMMA2, B3WC = range(7)
    BIAS_DOTS = ((CROSS + 1, 1), (CROSS + 1, 2), (CROSS + 2, 2),
                 (CROSS + 1, CROSS), (CROSS + 2, CROSS), (CROSS + 3, CROSS))
    SUMS = slice(P, P + B3WC + 1)

    def tables(k):
        return range(k * PER_CHUNK, min((k + 1) * PER_CHUNK, TABLES))

    def width(k):
        return P if k < FULL else LAST

    rows = emb.rearrange("t v e -> (t v) e")

    ctx = ExitStack()
    with ctx:
        def sb(name, shape, dt=fp32):
            return ctx.enter_context(nc.sbuf_tensor(name, shape, dt))

        def pb(name, shape):
            return ctx.enter_context(nc.psum_tensor(name, shape, fp32))

        def sem(name):
            return ctx.enter_context(nc.semaphore(name))

        cat_sb = sb("cat_sb", [P, TILES, TABLES], i32)
        num_sb = sb("num_sb", [P, TILES, NUMS])
        vec_rows = sb("vec_rows", [VECS, D])
        bias_rows = sb("bias_rows", [M1 + M2 + 2 * M3, P])
        w1_sb = sb("w1_sb", [P, CHUNKS, H1])
        w2_sb = sb("w2_sb", [P, M1, H2])
        w3_sb = sb("w3_sb", [P, M2, H3])
        wch_bc = sb("wch_bc", [P, H3])
        THREE = 96
        b2_rows = sb("b2_rows", [THREE, H2])
        b2_rest = sb("b2_rest", [THREE, H2])
        b2_rest2 = sb("b2_rest2", [THREE, H2])
        b2_cut = [sb(f"b2_cut{i}", [THREE, H2], bf16) for i in range(3)]
        b2_parts = sb("b2_parts", [THREE, H2], bf16)
        ones_bf = sb("ones_bf", [THREE, P], bf16)
        bc_bc = sb("bc_bc", [P, 1])
        ident = sb("ident", [P, P])
        ones = sb("ones", [P, P])
        table_base = sb("table_base", [P, TILES, TABLES])
        vecs = sb("vecs", [P, CHUNKS, VECS])
        bias_cols = sb("bias_cols", [P, M1 + M2 + 2 * M3])
        bias_prod = sb("bias_prod", [P, 7, CHUNKS])
        bias_part = sb("bias_part", [P, 7])
        cst = sb("cst", [P, 8])
        w3_prod = sb("w3_prod", [P, M2, H3])
        head = sb("head", [P, M2])
        head_diag = sb("head_diag", [P, M2, P])
        head_bc = sb("head_bc", [P, H2])
        clipped = sb("clipped", [P, TILES, TABLES])
        wrap = sb("wrap", [P, TILES, TABLES])
        idx_all = sb("idx_all", [P, TILES, TABLES], i32)
        idx = sb("idx", [P, PAIR, TABLES], i32)
        x = sb("x", [P, PAIR, D])
        xT = sb("xT", [P, CHUNKS, W])
        hT = sb("hT", [P, M1, W])
        relu2 = sb("relu2", [P, PAIR, H2])
        dots_sb = sb("dots_sb", [P, TILES, DOTS])
        p1 = sb("p1", [P, TILES])
        p2 = sb("p2", [P, TILES])
        p3 = sb("p3", [P, TILES])
        cross = sb("cross", [P, TILES])
        crossed = sb("crossed", [P, TILES])
        deep = sb("deep", [P, TILES])
        logit = sb("logit", [P, TILES])
        prob = sb("prob", [P, TILES])

        acc1 = pb("acc1", [P, M1, W])
        turned = pb("turned", [P, 512])
        dots = pb("dots", [P, 512])
        acc2 = pb("acc2", [P, PAIR, H2])
        BANK = 512
        M_PER_BANK = BANK // W
        BANKS1 = M1 // M_PER_BANK

        cat_in = sem("cat_in")
        num_in = sem("num_in")
        vec_in = sem("vec_in")
        bias_in = sem("bias_in")
        fold_in = sem("fold_in")
        w1_in = [sem(f"w1_in{k}") for k in range(CHUNKS)]
        w2_in = sem("w2_in")
        const_set = sem("const_set")
        ident_set = sem("ident_set")
        idx_step = sem("idx_step")
        idx_staged = sem("idx_staged")
        chunks_begun = sem("chunks_begun")
        all_idx = sem("all_idx")
        vecs_zero = sem("vecs_zero")
        vecs_turned = sem("vecs_turned")
        biases_ready = sem("biases_ready")
        fold_step = sem("fold_step")
        bias_part_ready = sem("bias_part_ready")
        bias_dots_done = sem("bias_dots_done")
        diag_ready = sem("diag_ready")
        head_turned = sem("head_turned")
        landed = [sem(f"landed{k}") for k in range(CHUNKS)]
        landed_last = [sem(f"landed_last{k}") for k in range(CHUNKS)]
        num_staged = sem("num_staged")
        transposed = sem("transposed")
        xT_ready = sem("xT_ready")
        l1_done = sem("l1_done")
        h_ready = sem("h_ready")
        dots_done = sem("dots_done")
        dots_read = sem("dots_read")
        cst_ready = sem("cst_ready")
        b2_step = sem("b2_step")
        b2_ready = sem("b2_ready")
        cross_step = sem("cross_step")
        l2_done = sem("l2_done")
        acc2_read = sem("acc2_read")
        logit_ready = sem("logit_ready")
        prob_ready = sem("prob_ready")
        stored = sem("stored")

        block = ctx.enter_context(nc.Block())

        LOOPS = PAIRS - 1

        @block.sync
        def _(sp):
            sp.dma_start(cat_sb[:, :, :], cat.rearrange("(p t) c -> p t c", p=P)).then_inc(cat_in, 16)
            sp.dma_start(wch_bc[:, :], Wc[D:D + H3, :].rearrange("n o -> o n").to_broadcast([P, H3])).then_inc(fold_in, 16)
            sp.dma_start(w3_sb[:, :, :], W3.rearrange("(c p) n -> p c n", p=P)).then_inc(fold_in, 16)
            for k in range(CHUNKS):
                sp.dma_start(w1_sb[0:width(k), k, :], W1[k * P:k * P + width(k), :]).then_inc(w1_in[k], 16)
            sp.dma_start(w2_sb[:, :, :], W2.rearrange("(c p) n -> p c n", p=P)).then_inc(w2_in, 16)
            sp.wait_ge(prob_ready, 2)
            sp.dma_start(out.rearrange("(p t) o -> p (t o)", p=P), prob[:, :]).then_inc(stored, 16)
            sp.wait_ge(stored, 16)

        @block.gpsimd
        def _(pool):
            pool.memset(ident[:, :], 0.0).then_inc(const_set, 1)
            pool.iota(table_base[:, :, :], pattern=[[0, TILES], [VOCAB, TABLES]], base=0,
                      channel_multiplier=0, allow_small_or_imprecise_dtypes=True).then_inc(const_set, 1)
            pool.memset(ones[:, :], 1.0).then_inc(const_set, 1)
            pool.wait_ge(const_set, 3)
            pool.affine_select(out=ident[:, :], in_=ident[:, :], compare_op=ALU.not_equal, fill=1.0,
                               base=0, pattern=[[-1, P]], channel_multiplier=1).then_inc(ident_set, 1)

            def gather(k, j, done):
                for t in tables(k):
                    pool.indirect_dma_start(
                        out=x[:, j, t * EMB:(t + 1) * EMB], out_offset=None, in_=rows,
                        in_offset=bass.IndirectOffsetOnAxis(ap=idx[:, j, t:t + 1], axis=0),
                    ).then_inc(done, 16)

            with pool.Fori(0, LOOPS) as g:
                for k in range(CHUNKS):
                    pool.wait_ge(idx_staged, g * CHUNKS + (k + 1))
                    pool.sem_inc(chunks_begun, 1)
                    for j in range(PAIR):
                        gather(k, j, landed[k])
            for j, done in ((0, landed), (1, landed_last)):
                for k in range(CHUNKS):
                    pool.wait_ge(idx_staged, LOOPS * CHUNKS + k + 1)
                    gather(k, j, done[k])

        @block.scalar
        def _(act):
            act.dma_start(vec_rows[0:CROSS, :], alphas).then_inc(vec_in, 16)
            act.dma_start(vec_rows[CROSS:CROSS + 1, :], Wc[0:D, :].rearrange("n o -> o n")).then_inc(vec_in, 16)
            act.dma_start(vec_rows[CROSS + 1:VECS, :], cross_bias).then_inc(vec_in, 16)
            act.dma_start(bias_rows[0:M1, :], b1.rearrange("(m p) -> m p", p=P)).then_inc(bias_in, 16)
            act.dma_start(bias_rows[M1:M1 + M2, :], b2.rearrange("(m p) -> m p", p=P)).then_inc(bias_in, 16)
            act.dma_start(bias_rows[M1 + M2:M1 + M2 + M3, :], b3.rearrange("(m p) -> m p", p=P)).then_inc(bias_in, 16)
            act.dma_start(bias_rows[M1 + M2 + M3:M1 + M2 + 2 * M3, :],
                          Wc[D:D + H3, :].rearrange("(m p) o -> m (p o)", p=P)).then_inc(bias_in, 16)
            act.dma_start(num_sb[:, :, :], num.rearrange("(p t) c -> p t c", p=P)).then_inc(num_in, 16)
            act.dma_start(b2_rows[:, :], b2.rearrange("(o n) -> o n", o=1).to_broadcast([THREE, H2])).then_inc(fold_in, 16)
            act.dma_start(bc_bc[:, :], bc.rearrange("(o n) -> o n", o=1).to_broadcast([P, 1])).then_inc(fold_in, 16)

            act.wait_ge(head_turned, 1)
            act.activation(head_bc[:, :], acc2[:, 1, :], ACT.Copy).then_inc(acc2_read, 1)
            act.wait_ge(num_in, 16)

            def stage_numbers(g):
                act.activation(x[:, :, TABLES * EMB:D], num_sb[:, bass.ds(g * PAIR, PAIR), :], ACT.Copy).then_inc(num_staged, 1)

            def relu1(base, lo, hi):
                for m in range(M1):
                    if m % M_PER_BANK == 0:
                        act.wait_ge(l1_done, base + (m // M_PER_BANK + 1))
                    act.activation(hT[:, m, lo:hi], acc1[:, m, lo:hi], ACT.Relu,
                                   bias=bias_cols[:, m:m + 1]).then_inc(h_ready, 1)

            act.wait_ge(biases_ready, 1)
            with act.Fori(0, LOOPS) as g:
                stage_numbers(g)
                relu1(g * BANKS1, 0, W)
            stage_numbers(LOOPS)
            for j in range(PAIR):
                relu1((LOOPS + j) * BANKS1, j * P, (j + 1) * P)
            act.wait_ge(logit_ready, 1)
            act.activation(prob[:, 0:TILES - 1], logit[:, 0:TILES - 1], ACT.Sigmoid).then_inc(prob_ready, 1)
            act.wait_ge(acc2_read, TILES + 1)
            act.activation(prob[:, TILES - 1:TILES], deep[:, TILES - 1:TILES], ACT.Sigmoid,
                           bias=crossed[:, TILES - 1:TILES]).then_inc(prob_ready, 1)

        @block.tensor
        def _(pe):
            pe.wait_ge(ident_set, 1)
            pe.wait_ge(vec_in, 3 * 16)
            pe.wait_ge(bias_in, 4 * 16)
            for k in range(CHUNKS):
                pe.transpose(acc2[0:width(k), 0, k * VECS:(k + 1) * VECS],
                             vec_rows[:, k * P:k * P + width(k)], ident[0:VECS, 0:VECS])
            n = bias_rows.shape[0]
            pe.transpose(acc2[:, 0, CHUNKS * VECS:CHUNKS * VECS + n], bias_rows[:, :], ident[0:n, 0:n]).then_inc(vecs_turned, 1)
            pe.wait_ge(bias_part_ready, 1)
            pe.matmul(acc2[:, 0, SUMS], ones[:, :], bias_part[:, :], start=True, stop=True).then_inc(bias_dots_done, 1)
            pe.wait_ge(diag_ready, M2)
            for c in range(M2):
                mm = pe.matmul(acc2[:, 1, c * P:(c + 1) * P], ones[:, :], head_diag[:, c, :], start=True, stop=True)
            mm.then_inc(head_turned, 1)
            for k in range(CHUNKS):
                pe.wait_ge(w1_in[k], 16)
            pe.wait_ge(w2_in, 16)
            pe.wait_ge(b2_ready, 3)

            def turn(k, tiles):
                for j in tiles:
                    mm = pe.transpose(turned[0:width(k), j * P:(j + 1) * P],
                                      x[:, j, k * P:k * P + width(k)], ident[:, :])
                mm.then_inc(transposed, 1)

            def layer1(k, tiles, r, first=False):
                lo, hi = tiles[0] * P, (tiles[-1] + 1) * P
                pe.wait_ge(xT_ready, r * CHUNKS + (k + 1))
                for m in range(M1):
                    if k == 0 and m % M_PER_BANK == 0 and not first:
                        pe.wait_ge(h_ready, (r - 1) * M1 + (m + M_PER_BANK))
                    mm = pe.matmul(acc1[:, m, lo:hi], w1_sb[0:width(k), k, m * P:(m + 1) * P],
                                   xT[0:width(k), k, lo:hi], start=(k == 0 and m % M_PER_BANK == 0),
                                   stop=(k == CHUNKS - 1), skip_group_check=True)
                    if k == CHUNKS - 1 and (m + 1) % M_PER_BANK == 0:
                        mm.then_inc(l1_done, 1)

            def cross_dots(k, tiles, r, first=False):
                if k == 0 and not first:
                    pe.wait_ge(dots_read, r)
                for j in tiles:
                    mm = pe.matmul(dots[:, j * DOTS:(j + 1) * DOTS], xT[0:width(k), k, j * P:(j + 1) * P],
                                   vecs[0:width(k), k, 0:DOTS], start=(k == 0 and j == tiles[0]),
                                   stop=(k == CHUNKS - 1), skip_group_check=True)
                if k == CHUNKS - 1:
                    mm.then_inc(dots_done, 1)

            L2_STEPS = 1 + M1

            def layer2(steps, tiles, r, tiles_read):
                for step in steps:
                    j, m = tiles[step // L2_STEPS], step % L2_STEPS - 1
                    if m < 0:
                        pe.wait_ge(acc2_read, tiles_read + 1)
                        pe.matmul(acc2[:, j, :], ones_bf[:, :], b2_parts[:, :], start=True, stop=False)
                        continue
                    pe.wait_ge(h_ready, r * M1 + (m + 1))
                    mm = pe.matmul(acc2[:, j, :], hT[:, m, j * P:(j + 1) * P], w2_sb[:, m, :],
                                   start=False, stop=(m == M1 - 1))
                    if m == M1 - 1:
                        mm.then_inc(l2_done, 1)

            def steps_beside(k, tiles):
                n = len(tiles) * L2_STEPS
                cut = [-(-n * i // (CHUNKS - 1)) for i in range(CHUNKS)] + [n]
                return range(cut[k], cut[k + 1])

            both = range(PAIR)
            pe.wait_ge(cst_ready, 1)
            pe.wait_ge(acc2_read, 1)
            for k in range(CHUNKS):
                pe.wait_ge(landed[k], 16 * PAIR * len(tables(k)))
                if k == CHUNKS - 1:
                    pe.wait_ge(num_staged, 1)
                turn(k, both)
                layer1(k, both, 0, first=True)
                cross_dots(k, both, 0, first=True)
            with pe.Fori(1, LOOPS) as g:
                for k in range(CHUNKS):
                    pe.wait_ge(landed[k], (g + 1) * (16 * PAIR * len(tables(k))))
                    if k == CHUNKS - 1:
                        pe.wait_ge(num_staged, g + 1)
                    turn(k, both)
                    layer2(steps_beside(k, both), both, g - 1, (g - 1) * PAIR)
                    layer1(k, both, g)
                    cross_dots(k, both, g)
            for k in range(CHUNKS):
                pe.wait_ge(landed[k], (LOOPS * PAIR + 1) * 16 * len(tables(k)))
                if k == CHUNKS - 1:
                    pe.wait_ge(num_staged, PAIRS)
                turn(k, [0])
                layer2(steps_beside(k, both), both, LOOPS - 1, (LOOPS - 1) * PAIR)
                layer1(k, [0], LOOPS)
                cross_dots(k, [0], LOOPS)
            for k in range(CHUNKS):
                pe.wait_ge(landed_last[k], 16 * len(tables(k)))
                turn(k, [1])
                layer2(steps_beside(k, [0]), [0], LOOPS, LOOPS * PAIR)
                if k == CHUNKS - 2:
                    layer2(range(0, 1), [1], LOOPS + 1, LOOPS * PAIR)
                layer1(k, [1], LOOPS + 1)
                if k == CHUNKS - 1:
                    layer2(range(1, 3), [1], LOOPS + 1, LOOPS * PAIR)
                cross_dots(k, [1], LOOPS + 1)
            layer2(range(3, L2_STEPS), [1], LOOPS + 1, LOOPS * PAIR)

        @block.vector
        def _(dve):
            dve.wait_ge(cat_in, 16)
            dve.wait_ge(const_set, 3)
            steps = 0
            for t0, t1 in ((0, PAIR), (PAIR, TILES)):
                c, w, b = (a[:, t0:t1, :] for a in (clipped, wrap, table_base))
                nc.vector.tensor_scalar(c, cat_sb[:, t0:t1, :], float(VOCAB - 1), float(-VOCAB),
                                        ALU.min, ALU.max).then_inc(idx_step, 1)
                steps += 1
                dve.wait_ge(idx_step, steps)
                nc.vector.tensor_scalar(w, c, 0.0, float(VOCAB), ALU.is_lt, ALU.mult).then_inc(idx_step, 1)
                nc.vector.tensor_tensor(c, c, b, ALU.add).then_inc(idx_step, 1)
                steps += 2
                dve.wait_ge(idx_step, steps)
                if t0 == 0:
                    for k in range(CHUNKS):
                        part = slice(tables(k)[0], tables(k)[-1] + 1)
                        nc.vector.tensor_tensor(idx[:, :, part], c[:, :, part], w[:, :, part],
                                                ALU.add).then_inc(idx_staged, 1)
                else:
                    nc.vector.tensor_tensor(idx_all[:, t0:t1, :], c, w, ALU.add).then_inc(all_idx, 1)

            nc.vector.memset(vecs[:, :, :], 0.0).then_inc(vecs_zero, 1)
            nc.vector.memset(bias_prod[:, :, :], 0.0).then_inc(vecs_zero, 1)
            dve.wait_ge(vecs_zero, 2)
            dve.wait_ge(vecs_turned, 1)
            turned_vecs = acc2[:, 0, 0:CHUNKS * VECS].rearrange("p (k v) -> p k v", v=VECS)
            nc.vector.tensor_copy(vecs[:, 0:FULL, :], turned_vecs[:, 0:FULL, :]).then_inc(fold_step, 1)
            nc.vector.tensor_copy(vecs[0:LAST, FULL, :], turned_vecs[0:LAST, FULL, :]).then_inc(fold_step, 1)
            nc.vector.tensor_copy(bias_cols[:, :], acc2[:, 0, CHUNKS * VECS:CHUNKS * VECS + bias_rows.shape[0]]).then_inc(biases_ready, 1)
            dve.wait_ge(fold_step, 2)
            dve.wait_ge(biases_ready, 1)
            for i, (u, v) in enumerate(BIAS_DOTS):
                nc.vector.tensor_tensor(bias_prod[:, i, :], vecs[:, :, u], vecs[:, :, v], ALU.mult).then_inc(fold_step, 1)
            nc.vector.tensor_tensor(bias_prod[:, B3WC, 0:M3], bias_cols[:, M1 + M2:M1 + M2 + M3],
                                    bias_cols[:, M1 + M2 + M3:M1 + M2 + 2 * M3], ALU.mult).then_inc(fold_step, 1)
            dve.wait_ge(fold_step, 9)
            nc.vector.tensor_reduce(bias_part[:, :], bias_prod[:, :, :], AX.X, ALU.add).then_inc(bias_part_ready, 1)
            dve.wait_ge(fold_in, 4 * 16)
            nc.vector.tensor_tensor(w3_prod[:, :, :], w3_sb[:, :, :],
                                    wch_bc[:, None, :].to_broadcast([P, M2, H3]), ALU.mult).then_inc(fold_step, 1)
            dve.wait_ge(fold_step, 10)
            nc.vector.tensor_reduce(head[:, :], w3_prod[:, :, :], AX.X, ALU.add).then_inc(fold_step, 1)
            dve.wait_ge(fold_step, 11)
            dve.wait_ge(ident_set, 1)
            for c in range(M2):
                nc.vector.tensor_scalar(head_diag[:, c, :], ident[:, :], head[:, c:c + 1], None,
                                        ALU.mult).then_inc(diag_ready, 1)
            dve.wait_ge(bias_dots_done, 1)
            nc.vector.tensor_copy(cst[:, 0:7], acc2[:, 0, SUMS]).then_inc(fold_step, 1)
            dve.wait_ge(fold_step, 12)
            nc.vector.scalar_tensor_tensor(cst[:, 7:8], cst[:, GAMMA2:GAMMA2 + 1], cst[:, B3WC:B3WC + 1],
                                           bc_bc[:, :], ALU.add, ALU.add).then_inc(cst_ready, 1)
            nc.vector.memset(b2_parts[:, :], 0.0).then_inc(b2_step, 1)
            nc.vector.memset(ones_bf[:, :], 1.0).then_inc(b2_step, 1)
            nc.vector.tensor_copy(b2_cut[0][:, :], b2_rows[:, :]).then_inc(b2_step, 1)
            dve.wait_ge(b2_step, 3)
            nc.vector.tensor_tensor(b2_rest[:, :], b2_rows[:, :], b2_cut[0][:, :], ALU.subtract).then_inc(b2_step, 1)
            dve.wait_ge(b2_step, 4)
            nc.vector.tensor_copy(b2_cut[1][:, :], b2_rest[:, :]).then_inc(b2_step, 1)
            dve.wait_ge(b2_step, 5)
            nc.vector.tensor_tensor(b2_rest2[:, :], b2_rest[:, :], b2_cut[1][:, :], ALU.subtract).then_inc(b2_step, 1)
            dve.wait_ge(b2_step, 6)
            nc.vector.tensor_copy(b2_cut[2][:, :], b2_rest2[:, :]).then_inc(b2_step, 1)
            dve.wait_ge(b2_step, 7)
            for i in range(3):
                nc.vector.tensor_copy(b2_parts[32 * i:32 * i + 1, :], b2_cut[i][32 * i:32 * i + 1, :]).then_inc(b2_ready, 1)
            dve.wait_ge(all_idx, 1)
            dve.wait_ge(cst_ready, 1)
            dve.wait_ge(acc2_read, 1)

            def const(i):
                return cst[:, i:i + 1]

            def deep_share(j, t):
                dve.wait_ge(l2_done, t + 1)
                nc.vector.scalar_tensor_tensor(relu2[:, j, :], acc2[:, j, :], 0.0, head_bc[:, :], ALU.max, ALU.mult,
                                               accum_out=deep[:, bass.ds(t, 1)]).then_inc(acc2_read, 1)

            def follow(tiles, r, t_at, next_pair, shares):
                lo, hi = tiles[0] * P, (tiles[-1] + 1) * P
                for k in range(CHUNKS):
                    dve.wait_ge(transposed, r * CHUNKS + (k + 1))
                    nc.vector.tensor_copy(xT[0:width(k), k, lo:hi], turned[0:width(k), lo:hi]).then_inc(xT_ready, 1)
                    if next_pair is not None:
                        part = slice(tables(k)[0], tables(k)[-1] + 1)
                        nc.vector.tensor_copy(idx[:, :, part], idx_all[:, bass.ds(next_pair * PAIR, PAIR), part]).then_inc(idx_staged, 1)
                    if k in shares:
                        deep_share(*shares[k])
                dve.wait_ge(dots_done, r + 1)
                nc.vector.tensor_copy(dots_sb[:, bass.ds(t_at, len(tiles)), :],
                                      dots[:, 0:PAIR * DOTS].rearrange("p (j d) -> p j d", d=DOTS)[:, tiles[0]:tiles[-1] + 1, :],
                                      ).then_inc(dots_read, 1)

            def pair_shares(pair):
                return {CHUNKS // 2: (0, pair * PAIR), CHUNKS - 1: (1, pair * PAIR + 1)}

            both = range(PAIR)
            follow(both, 0, 0, 1, {})
            with dve.Fori(1, LOOPS) as g:
                follow(both, g, g * PAIR, g + 1, pair_shares(g - 1))
            follow([0], LOOPS, LOOPS * PAIR, None, pair_shares(LOOPS - 1))
            follow([1], LOOPS + 1, LOOPS * PAIR + 1, None, {CHUNKS - 1: (0, LOOPS * PAIR)})

            dot = [dots_sb[:, :, d] for d in range(DOTS)]
            q1, q2, q3, q = (a[:, :] for a in (p1, p2, p3, cross))
            dve.wait_ge(dots_read, LOOPS + PAIR)
            nc.vector.tensor_scalar(q1, dot[0], 1.0, None, ALU.add).then_inc(cross_step, 1)
            dve.wait_ge(cross_step, 1)
            nc.vector.tensor_tensor(q2, dot[1], q1, ALU.mult).then_inc(cross_step, 1)
            nc.vector.tensor_tensor(q3, dot[2], q1, ALU.mult).then_inc(cross_step, 1)
            nc.vector.tensor_tensor(q, dot[3], q1, ALU.mult).then_inc(cross_step, 1)
            dve.wait_ge(cross_step, 4)
            nc.vector.tensor_scalar(q2, q2, const(BETA01), 1.0, ALU.add, ALU.add).then_inc(cross_step, 1)
            dve.wait_ge(cross_step, 5)
            nc.vector.scalar_tensor_tensor(q3, q3, const(BETA02), q2, ALU.add, ALU.mult).then_inc(cross_step, 1)
            nc.vector.scalar_tensor_tensor(q, q, const(GAMMA0), q2, ALU.add, ALU.mult).then_inc(cross_step, 1)
            dve.wait_ge(cross_step, 7)
            nc.vector.tensor_scalar(q3, q3, const(BETA12), 1.0, ALU.add, ALU.add).then_inc(cross_step, 1)
            dve.wait_ge(cross_step, 8)
            nc.vector.scalar_tensor_tensor(q, q, const(GAMMA1), q3, ALU.add, ALU.mult).then_inc(cross_step, 1)
            dve.wait_ge(cross_step, 9)
            nc.vector.tensor_scalar(crossed[:, :], q, const(7), None, ALU.add).then_inc(cross_step, 1)
            dve.wait_ge(cross_step, 10)
            dve.wait_ge(acc2_read, TILES)
            nc.vector.tensor_tensor(logit[:, 0:TILES - 1], crossed[:, 0:TILES - 1], deep[:, 0:TILES - 1],
                                    ALU.add).then_inc(logit_ready, 1)
            deep_share(1, TILES - 1)


_PREFIX = "L0_rec_"
_INS = ["r_categorical_input"] + [_PREFIX + n for n in (
    "numerical_input", "emb_tables", "alphas", "cross_bias", "W1", "b1", "W2", "b2", "W3", "b3", "Wc", "bc")]


def kernel(**inputs):
    import numpy as _np
    import concourse.bacc as _bacc
    from concourse import mybir as _mybir
    from concourse.bass_utils import run_bass_kernel_spmd as _run

    nc = _bacc.Bacc("TRN2", target_bir_lowering=False, num_devices=1)
    arrays, args = {}, []
    for name in _INS:
        a = _np.ascontiguousarray(inputs[name])
        arrays[f"in_{name}_dram"] = a
        args.append(nc.dram_tensor(f"in_{name}_dram", a.shape, _mybir.dt.from_np(a.dtype), kind="ExternalInput").ap())
    shape = (inputs["r_categorical_input"].shape[0], inputs[_PREFIX + "Wc"].shape[1])
    args.append(nc.dram_tensor("out_dram", shape, _mybir.dt.float32, kind="ExternalOutput").ap())
    deep_cross_kernel(nc, *args)
    r = _run(nc, [arrays], core_ids=[0])
    return r.results[0]["out_dram"]
```
